# Optimizing a Trainium2 kernel written in Bass

```python
import numpy as np
import jax
import jax.numpy as jnp

def _softmax(x, axis=-1):
    return jax.nn.softmax(x, axis=axis)

def _gelu(x):
    return jax.nn.gelu(x, approximate=True)

def _silu(x):
    return jax.nn.silu(x)

def _sigmoid(x):
    return jax.nn.sigmoid(x)

def _layernorm(x, axis=-1, eps=1e-05):
    m = jnp.mean(x, axis=axis, keepdims=True)
    v = jnp.var(x, axis=axis, keepdims=True)
    return (x - m) / jnp.sqrt(v + eps)

def _scatter_add(tgt, idx, src, axis=0):
    return tgt.at[idx].add(src)

def _segment_sum(src, seg, n):
    return jax.ops.segment_sum(src, seg, n)
kernel_name = 'mk_adj_resnorm_d1_adj_r2_239278'

def setup_inputs(seed: int=0):
    np.random.seed(seed)
    _w = jnp.asarray

    def _rec_inputs():
        import jax
        import jax.numpy as jnp
        _gk = jax.random.key(seed)
        x = -0.0002928 + 1 * jax.random.normal(jax.random.fold_in(_gk, 1), (2048, 256), jnp.float32)
        _a = jax.random.bernoulli(jax.random.fold_in(_gk, 2), 0.00390625, (2048, 2048))
        _a = jnp.logical_or(_a, jnp.swapaxes(_a, -1, -2))
        _a = jnp.logical_or(_a, jnp.eye(2048, dtype=bool))
        _af = _a.astype(jnp.float32)
        _af = _af * jax.random.uniform(jax.random.fold_in(_gk, 3), (2048, 2048), jnp.float32, 0.05, 0.0541998)
        adj = _af
        return (x, adj)
    x, adj = _rec_inputs()

    def _L0_gnn_setup():
        import jax, jax.numpy as jnp
        import numpy as np
        import math
        N = 4096
        D_IN = 256
        D_H = 256

        def _layer(x, cooccur, wq, bq, wk, bk, wv, bv, scale):
            q = x @ wq.T + bq
            k = x @ wk.T + bk
            v = x @ wv.T + bv
            att = jax.nn.softmax(jnp.einsum('ac,bc->ab', q, k) * scale, axis=-1)
            att = att + cooccur
            return jax.nn.relu(att @ v)
        key = jax.random.key(seed)
        ks = jax.random.split(key, 18)
        s_in = 1.0 / math.sqrt(D_IN)
        s_h = 1.0 / math.sqrt(D_H)
        f32 = jnp.float32
        return {'x': jax.random.normal(ks[0], (N, D_IN), dtype=f32), 'cooccur': jax.random.normal(ks[1], (N, N), dtype=f32) * 0.01, 'wq0': jax.random.normal(ks[2], (D_H, D_IN), dtype=f32) * s_in, 'bq0': jnp.zeros((D_H,), dtype=f32), 'wk0': jax.random.normal(ks[3], (D_H, D_IN), dtype=f32) * s_in, 'bk0': jnp.zeros((D_H,), dtype=f32), 'wv0': jax.random.normal(ks[4], (D_H, D_IN), dtype=f32) * s_in, 'bv0': jnp.zeros((D_H,), dtype=f32), 'wres': jax.random.normal(ks[5], (D_H, D_IN), dtype=f32) * s_in, 'bres': jnp.zeros((D_H,), dtype=f32), 'wq1': jax.random.normal(ks[6], (D_H, D_H), dtype=f32) * s_h, 'bq1': jnp.zeros((D_H,), dtype=f32), 'wk1': jax.random.normal(ks[7], (D_H, D_H), dtype=f32) * s_h, 'bk1': jnp.zeros((D_H,), dtype=f32), 'wv1': jax.random.normal(ks[8], (D_H, D_H), dtype=f32) * s_h, 'bv1': jnp.zeros((D_H,), dtype=f32)}
    _L0_gnn_all = _L0_gnn_setup()
    _L0_gnn_in = {k: v for k, v in _L0_gnn_all.items() if k in ('wq0', 'bq0', 'wk0', 'bk0', 'wv0', 'bv0', 'wres', 'bres', 'wq1', 'bq1', 'wk1', 'bk1', 'wv1', 'bv1')}
    del _L0_gnn_all
    return {'x': x, 'adj': adj, 'L0_gnn_wq0': _L0_gnn_in['wq0'], 'L0_gnn_bq0': _L0_gnn_in['bq0'], 'L0_gnn_wk0': _L0_gnn_in['wk0'], 'L0_gnn_bk0': _L0_gnn_in['bk0'], 'L0_gnn_wv0': _L0_gnn_in['wv0'], 'L0_gnn_bv0': _L0_gnn_in['bv0'], 'L0_gnn_wres': _L0_gnn_in['wres'], 'L0_gnn_bres': _L0_gnn_in['bres'], 'L0_gnn_wq1': _L0_gnn_in['wq1'], 'L0_gnn_bq1': _L0_gnn_in['bq1'], 'L0_gnn_wk1': _L0_gnn_in['wk1'], 'L0_gnn_bk1': _L0_gnn_in['bk1'], 'L0_gnn_wv1': _L0_gnn_in['wv1'], 'L0_gnn_bv1': _L0_gnn_in['bv1']}

def reference(x, adj, L0_gnn_wq0, L0_gnn_bq0, L0_gnn_wk0, L0_gnn_bk0, L0_gnn_wv0, L0_gnn_bv0, L0_gnn_wres, L0_gnn_bres, L0_gnn_wq1, L0_gnn_bq1, L0_gnn_wk1, L0_gnn_bk1, L0_gnn_wv1, L0_gnn_bv1):
    import jax
    import jax.numpy as jnp

    def _L0_gnn_ref(x, cooccur, wq0, bq0, wk0, bk0, wv0, bv0, wres, bres, wq1, bq1, wk1, bk1, wv1, bv1):
        import jax, jax.numpy as jnp
        import numpy as np
        import math
        N = 4096
        D_IN = 256
        D_H = 256

        def _layer(x, cooccur, wq, bq, wk, bk, wv, bv, scale):
            q = x @ wq.T + bq
            k = x @ wk.T + bk
            v = x @ wv.T + bv
            att = jax.nn.softmax(jnp.einsum('ac,bc->ab', q, k) * scale, axis=-1)
            att = att + cooccur
            return jax.nn.relu(att @ v)
        scale = 1.0 / math.sqrt(D_H)
        x = _layer(x, cooccur, wq0, bq0, wk0, bk0, wv0, bv0, scale) + (x @ wres.T + bres)
        x = _layer(x, cooccur, wq1, bq1, wk1, bk1, wv1, bv1, scale) + x
        return x
    x = _layernorm(x + _L0_gnn_ref(x, adj, L0_gnn_wq0, L0_gnn_bq0, L0_gnn_wk0, L0_gnn_bk0, L0_gnn_wv0, L0_gnn_bv0, L0_gnn_wres, L0_gnn_bres, L0_gnn_wq1, L0_gnn_bq1, L0_gnn_wk1, L0_gnn_bk1, L0_gnn_wv1, L0_gnn_bv1), axis=-1)
    return x

_drawn_inputs = setup_inputs


def setup_inputs(seed=0):
    import zlib

    import numpy as np

    out = dict(_drawn_inputs(seed))
    spreads = {'L0_gnn_bq0': (0.0, 0.8),
     'L0_gnn_bk0': (0.0, 0.8),
     'L0_gnn_bv0': (0.0, 0.1),
     'L0_gnn_bres': (0.0, 0.1),
     'L0_gnn_bq1': (0.0, 0.8),
     'L0_gnn_bk1': (0.0, 0.8),
     'L0_gnn_bv1': (0.0, 0.1)}
    factors = {}
    for name, (base, spread) in spreads.items():
        noise = np.random.default_rng([zlib.crc32(name.encode()), seed]).standard_normal(out[name].shape)
        drawn = base * np.exp(spread * noise) if base else spread * noise
        out[name] = jnp.asarray(drawn.astype(out[name].dtype))
    for name, factor in factors.items():
        out[name] = (out[name] * factor).astype(out[name].dtype)
    return out
```

```python
from contextlib import ExitStack

import concourse.bass as bass
from concourse import mybir
from concourse.alu_op_type import AluOpType as ALU

F32 = mybir.dt.float32
F32R = mybir.dt.float32r
ACT = mybir.ActivationFunctionType
AX = mybir.AxisListType

P = 128
N = 2048
D = 256
CC = D // P
TILES = N // P
PAIRS = TILES // 2
PAIR = 2 * P
BANK = 512
ROUNDS = N // BANK
BLOCKS = BANK // P
LAYERS = 2
DMA = 16
EPS = 1e-5
Q_SCALE = D ** -0.5
PARTS = ((0, 0), (1, 0), (0, 1))
WQ, WK, WV, WRES = range(4)


def two_layer_attention(nc, x, xT, adj, weights, cols, rows, ident_in, out):
    with ExitStack() as ctx:
        def sb(name, shape, dt=F32):
            return ctx.enter_context(nc.sbuf_tensor(name, shape, dt))

        def sem(name):
            return ctx.enter_context(nc.semaphore(name))

        x_t = sb("x_t", [P, CC, N])
        q_all = sb("q_all", [P, CC, N])
        k_hl = sb("k_hl", [P, 2, CC, N], F32R)
        v_hl = sb("v_hl", [P, 2, TILES * D], F32R)
        x1 = sb("x1", [P, TILES * D])
        w_hl = sb("w_hl", [P, 2, 4, CC, D], F32R)
        mixT = sb("mixT", [P, 2, 2, TILES, P], F32R)
        probs = sb("probs", [P, 2, N])
        adj_sb = sb("adj_sb", [P, 2, N])
        ident = sb("ident", [P, P])
        q_hl = sb("q_hl", [P, 2, 2, CC, P], F32R)
        x_row = sb("x_row", [P, 2, D])
        y = sb("y", [P, 2, D])
        y_norm = sb("y_norm", [P, 2, D])
        b_col = sb("b_col", [P, LAYERS, 2, CC])
        bq_scaled = sb("bq_scaled", [P, LAYERS, CC])
        b_row = sb("b_row", [P, 3, D])
        chunk_max = sb("chunk_max", [P, 2, ROUNDS])
        neg_max = sb("neg_max", [P, 2])
        row_sum = sb("row_sum", [P, 2])
        inv_sum = sb("inv_sum", [P, 2])
        stats = sb("stats", [P, 2, 6])
        mean_var = sb("mean_var", [P, 2, 2])
        var_eps = sb("var_eps", [P, 2])
        inv_std = sb("inv_std", [P, 2])
        minus_half = sb("minus_half", [P, 1])
        eps = sb("eps", [P, 1])

        x_hl = mixT[:, :, :, 0:2 * CC, :].rearrange("p s h (c t) a -> p s h c (t a)", c=CC)
        v_sum = probs[:, 0, 0:2 * PAIR * 2].rearrange("p (s n) -> p s n", s=2)
        w_raw = probs[:, 1, :].rearrange("p (w c n) -> p w c n", w=4, c=CC)

        psum = ctx.enter_context(nc.psum_tensor("psum", [P, 8, BANK], F32))
        scores_ps = psum[:, 0:ROUNDS, :]
        turned_ps = psum[:, ROUNDS:ROUNDS + 2, :]
        mixed_ps = psum[:, 6, 0:D]
        x1T_ps = psum[:, 7, 0:D]

        w_loaded = [sem(f"w_loaded{i}") for i in range(4)]
        b_loaded = sem("b_loaded")
        w_hi_done, w_lo_done = sem("w_hi_done"), sem("w_lo_done")
        bq_done = sem("bq_done")
        x_loaded = [sem(f"x_loaded{i}") for i in range(2)]
        x_hi_done, x_lo_done = sem("x_hi_done"), sem("x_lo_done")
        q_made, k_made, v_made, r_made = (sem(f"{n}_made") for n in "qkvr")
        q_kept, k_hi_kept = sem("q_kept"), sem("k_hi_kept")
        k_lo_kept, v_summed, r_kept = sem("k_lo_kept"), sem("v_summed"), sem("r_kept")
        v_hi_kept, v_lo_kept = sem("v_hi_kept"), sem("v_lo_kept")
        q_hi_ready, q_lo_ready = sem("q_hi_ready"), sem("q_lo_ready")
        scored = sem("scored")
        chunk_maxed, maxed = sem("chunk_maxed"), sem("maxed")
        exped = sem("exped")
        inverted = sem("inverted")
        adj_loaded = [sem(f"adj_loaded{i}") for i in range(2)]
        combined = sem("combined")
        turned = sem("turned")
        mix_hi, mix_lo = sem("mix_hi"), sem("mix_lo")
        mixed = sem("mixed")
        y_ready = sem("y_ready")
        x1_kept = sem("x1_kept")
        x1_turned = sem("x1_turned")
        x1T_kept = sem("x1T_kept")
        row_loaded = [sem(f"row_loaded{i}") for i in range(2)]
        x_added = sem("x_added")
        stats_made, moments_made = sem("stats_made"), sem("moments_made")
        eps_added, std_made = sem("eps_added"), sem("std_made")
        consts_made = sem("consts_made")
        normed = sem("normed")
        stored = [sem(f"stored{i}") for i in range(2)]

        block = ctx.enter_context(nc.Block())

        def over_pairs(eng, body):
            with eng.Fori(0, PAIRS // 2) as i:
                for par in range(2):
                    body(i * 2 + par, par)

        def over_steps(eng, step):
            def on(t):
                return {"tile": t < TILES, "previous": 1 <= t <= TILES,
                        "second": 2 <= t <= TILES + 1, "third": 3 <= t <= TILES + 2,
                        "next": t + 1 < TILES}
            for t in range(6):
                step(t, t % 2, on(t))
            with eng.Fori(3, TILES // 2 - 1) as i:
                for par in range(2):
                    step(i * 2 + par, par, on(6))
            for t in range(TILES - 2, TILES + 3):
                step(t, t % 2, on(t))

        @block.sync
        def _(sp):
            for w in range(4):
                sp.dma_start(w_raw[:, w], weights[0][w].rearrange("(c p) n -> p c n", p=P))\
                    .then_inc(w_loaded[w], DMA)
                if w == 0:
                    sp.dma_start(x_t[:, :, 0:PAIR], xT.rearrange("(c p) n -> p c n", p=P)[:, :, 0:PAIR])\
                        .then_inc(x_loaded[0], DMA)
            xT_v = xT.rearrange("(c p) n -> p c n", p=P)
            sp.dma_start(x_t[:, :, PAIR:2 * PAIR], xT_v[:, :, PAIR:2 * PAIR]).then_inc(x_loaded[1], DMA)
            with sp.Fori(1, PAIRS // 2) as i:
                for par in range(2):
                    cols_ = bass.ds((i * 2 + par) * PAIR, PAIR)
                    sp.wait_ge(x_loaded[par], i * DMA)
                    sp.dma_start(x_t[:, :, cols_], xT_v[:, :, cols_]).then_inc(x_loaded[par], DMA)
            for layer in range(LAYERS):
                for t in range(2):
                    if layer:
                        sp.wait_ge(combined, ROUNDS * (TILES + t - 1))
                    sp.dma_start(adj_sb[:, t], adj[t * P:(t + 1) * P, :]).then_inc(adj_loaded[t], DMA)
                if layer == 0:
                    sp.wait_ge(w_lo_done, 4)
                    for w in range(3):
                        sp.dma_start(w_raw[:, w], weights[1][w].rearrange("(c p) n -> p c n", p=P))\
                            .then_inc(w_loaded[w], DMA)
                with sp.Fori(1, TILES // 2) as i:
                    for par in range(2):
                        t = i * 2 + par
                        sp.wait_ge(combined, (t + (layer * TILES - 1)) * ROUNDS)
                        sp.dma_start(adj_sb[:, par], adj[bass.ds(t * P, P), :])\
                            .then_inc(adj_loaded[par], DMA)

        @block.gpsimd
        def _(pool):
            pool.memset(minus_half[:], -0.5).then_inc(consts_made, 1)
            pool.memset(eps[:], EPS).then_inc(consts_made, 1)

            def keep_v_lo(layer, p, par):
                m = p + layer * PAIRS
                pool.wait_ge(v_hi_kept, m + 1)
                at = bass.ds(p * (2 * D), 2 * D)
                pool.tensor_tensor(v_hl[:, 1, at], v_sum[:, par], v_hl[:, 0, at].bitcast(F32),
                                   ALU.subtract).then_inc(v_lo_kept, 1)

            def keep_x1(t, par):
                pool.wait_ge(y_ready, t + 1)
                pool.tensor_copy(x1[:, bass.ds(t * D, D)], y[:, par]).then_inc(x1_kept, 1)

            def norm_step(t, par):
                pool.wait_ge(y_ready, t + (TILES + 1))
                if isinstance(t, int):
                    pool.wait_ge(row_loaded[par], DMA * (t // 2 + 1))
                else:
                    pool.wait_ge(row_loaded[par], (t + (2 - par)) * (DMA // 2))
                pool.tensor_tensor(y[:, par], y[:, par], x_row[:, par], ALU.add).then_inc(x_added, 1)
                pool.wait_ge(moments_made, t + 1)
                pool.tensor_tensor(var_eps[:, par:par + 1], mean_var[:, par, 1:2], eps[:], ALU.add)\
                    .then_inc(eps_added, 1)
                pool.wait_ge(eps_added, t + 1)
                pool.tensor_tensor(inv_std[:, par:par + 1], var_eps[:, par:par + 1], minus_half[:],
                                   ALU.pow).then_inc(std_made, 1)

            over_pairs(pool, lambda p, par: keep_v_lo(0, p, par))
            with pool.Fori(0, TILES // 2) as i:
                for par in range(2):
                    keep_x1(i * 2 + par, par)
            over_pairs(pool, lambda p, par: keep_v_lo(1, p, par))
            pool.wait_ge(consts_made, 2)
            with pool.Fori(0, TILES // 2) as i:
                for par in range(2):
                    norm_step(i * 2 + par, par)

        @block.scalar
        def _(act):
            act.dma_start(b_col[:], cols).then_inc(b_loaded, DMA)
            act.dma_start(ident[:], ident_in).then_inc(b_loaded, DMA)
            for i, b in enumerate(rows):
                act.dma_start(b_row[:, i], b.partition_broadcast(P)).then_inc(b_loaded, DMA)

            def split_weights(layer, count):
                for w in range(count):
                    act.wait_ge(w_loaded[w], DMA * (layer + 1))
                    nc.scalar.activation(w_hl[:, 0, w], w_raw[:, w], ACT.Copy).then_inc(w_hi_done, 1)

            def split_x(layer, p, par):
                m = p + layer * PAIRS
                if layer == 0:
                    act.wait_ge(x_loaded[par], (p + (2 - par)) * (DMA // 2))
                else:
                    act.wait_ge(x1T_kept, p * 2 + 2)
                if not isinstance(p, int) or m >= 2:
                    act.wait_ge(k_made, m - 1)
                    act.wait_ge(q_made, m - 1)
                    act.wait_ge(v_made, m - 1)
                    if layer == 0:
                        act.wait_ge(r_made, m - 1)
                nc.scalar.activation(x_hl[:, par, 0], x_t[:, :, bass.ds(p * PAIR, PAIR)], ACT.Copy)\
                    .then_inc(x_hi_done, 1)

            def keep_projections(layer, p, par):
                m = p + layer * PAIRS
                at = bass.ds(p * PAIR, PAIR)
                bank = 4 * par
                act.wait_ge(k_made, m + 1)
                for cc in range(CC):
                    ins = nc.scalar.activation(k_hl[:, 0, cc, at], psum[:, bank + WK, cc * PAIR:(cc + 1) * PAIR],
                                               ACT.Identity, bias=b_col[:, layer, 1, cc:cc + 1])
                ins.then_inc(k_hi_kept, 1)
                act.wait_ge(q_made, m + 1)
                for cc in range(CC):
                    ins = nc.scalar.activation(q_all[:, cc, at], psum[:, bank + WQ, cc * PAIR:(cc + 1) * PAIR],
                                               ACT.Identity, bias=bq_scaled[:, layer, cc:cc + 1], scale=Q_SCALE)
                ins.then_inc(q_kept, 1)
                act.wait_ge(v_summed, m + 1)
                nc.scalar.activation(v_hl[:, 0, bass.ds(p * (2 * D), 2 * D)], v_sum[:, par], ACT.Copy)\
                    .then_inc(v_hi_kept, 1)

            def projections(layer):
                split_x(layer, 0, 0)
                split_x(layer, 1, 1)
                keep_projections(layer, 0, 0)
                split_x(layer, 2, 0)
                keep_projections(layer, 1, 1)
                split_x(layer, 3, 1)
                keep_projections(layer, 2, 0)
                with act.Fori(2, PAIRS // 2) as i:
                    split_x(layer, i * 2, 0)
                    keep_projections(layer, i * 2 - 1, 1)
                    split_x(layer, i * 2 + 1, 1)
                    keep_projections(layer, i * 2, 0)
                keep_projections(layer, PAIRS - 1, 1)

            def split_q(layer, t, par):
                n = t + layer * TILES
                if not isinstance(t, int) or n >= 2:
                    act.wait_ge(scored, (n - 1) * ROUNDS)
                nc.scalar.activation(q_hl[:, par, 0], q_all[:, :, bass.ds(t * P, P)], ACT.Copy)\
                    .then_inc(q_hi_ready, 1)

            def mix_hi_round(layer, t, par, j):
                n = t + layer * TILES
                act.wait_ge(turned, n * ROUNDS + (j + 1))
                if not isinstance(t, int) or n >= 2:
                    if j == 0:
                        act.wait_ge(mixed, n - 1)
                nc.scalar.activation(mixT[:, par, 0, BLOCKS * j:BLOCKS * (j + 1), :],
                                     turned_ps[:, j % 2, :].rearrange("p (k a) -> p k a", a=P),
                                     ACT.Copy).then_inc(mix_hi, 1)

            def step(layer, t, par, on):
                n = t + layer * TILES
                if layer == 1 and on["third"]:
                    if not isinstance(t, int) or t - 3 >= 2:
                        act.wait_ge(x_added, t - 4)
                    act.dma_start(x_row[:, 1 - par], x[bass.ds((t - 3) * P, P), :])\
                        .then_inc(row_loaded[1 - par], DMA)
                if layer == 1 and (not isinstance(t, int) or t >= 4):
                    store(t - 4, par)
                if on["previous"]:
                    mix_hi_round(layer, t - 1, 1 - par, 0)
                if on["tile"]:
                    act.wait_ge(maxed, n + 1)
                    if not isinstance(t, int) or n >= 2:
                        act.wait_ge(turned, (n - 1) * ROUNDS)
                    nc.scalar.activation(probs[:, par], scores_ps.rearrange("p j n -> p (j n)"), ACT.Exp,
                                         bias=neg_max[:, par:par + 1], scale=1.0,
                                         accum_out=row_sum[:, par:par + 1]).then_inc(exped, 1)
                if on["next"]:
                    split_q(layer, t + 1, 1 - par)
                if on["previous"]:
                    mix_hi_round(layer, t - 1, 1 - par, 1)
                if layer == 0 and on["third"]:
                    act.wait_ge(x1_turned, t - 2)
                    nc.scalar.activation(x_t[:, :, bass.ds((t - 3) * P, P)],
                                         x1T_ps.rearrange("p (c a) -> p c a", c=CC), ACT.Copy)\
                        .then_inc(x1T_kept, 1)
                if on["previous"]:
                    mix_hi_round(layer, t - 1, 1 - par, 2)
                    mix_hi_round(layer, t - 1, 1 - par, 3)

            def store(t, par):
                act.wait_ge(normed, t + 1)
                act.dma_start(out[bass.ds(t * P, P), :], y_norm[:, par]).then_inc(stored[par], DMA)

            act.wait_ge(b_loaded, 5 * DMA)
            split_weights(0, 4)
            act.wait_ge(bq_done, 1)
            for layer in range(LAYERS):
                if layer == 0:
                    pass
                else:
                    act.wait_ge(mixed, TILES)
                    act.wait_ge(q_lo_ready, TILES)
                projections(layer)
                act.wait_ge(v_lo_kept, PAIRS * (layer + 1))
                act.wait_ge(x_lo_done, PAIRS * (layer + 1))
                act.wait_ge(v_made, PAIRS * (layer + 1))
                act.wait_ge(r_made, PAIRS)
                split_q(layer, 0, 0)
                if layer == 0:
                    split_weights(1, 3)
                    act.wait_ge(w_lo_done, 7)
                over_steps(act, lambda t, par, on, layer=layer: step(layer, t, par, on))
            for t in range(TILES - 1, TILES):
                store(t, t % 2)
            for par in range(2):
                act.wait_ge(stored[par], DMA * (TILES // 2))

        @block.vector
        def _(dve):
            dve.wait_ge(b_loaded, 5 * DMA)
            nc.vector.tensor_scalar(bq_scaled[:], b_col[:, :, 0, :], Q_SCALE, None, ALU.mult)\
                .then_inc(bq_done, 1)

            def split_weights(layer, count):
                for w in range(count):
                    dve.wait_ge(w_hi_done, 4 * layer + w + 1)
                    nc.vector.tensor_tensor(w_hl[:, 1, w], w_raw[:, w], w_hl[:, 0, w].bitcast(F32),
                                            ALU.subtract).then_inc(w_lo_done, 1)

            def split_x(layer, p, par):
                m = p + layer * PAIRS
                dve.wait_ge(x_hi_done, m + 1)
                nc.vector.tensor_tensor(x_hl[:, par, 1], x_t[:, :, bass.ds(p * PAIR, PAIR)],
                                        x_hl[:, par, 0].bitcast(F32), ALU.subtract).then_inc(x_lo_done, 1)

            def keep_projections(layer, p, par):
                m = p + layer * PAIRS
                at = bass.ds(p * PAIR, PAIR)
                bank = 4 * par
                dve.wait_ge(k_hi_kept, m + 1)
                for cc in range(CC):
                    ins = nc.vector.scalar_tensor_tensor(
                        k_hl[:, 1, cc, at], psum[:, bank + WK, cc * PAIR:(cc + 1) * PAIR],
                        b_col[:, layer, 1, cc:cc + 1], k_hl[:, 0, cc, at].bitcast(F32),
                        ALU.add, ALU.subtract)
                ins.then_inc(k_lo_kept, 1)
                dve.wait_ge(v_made, m + 1)
                if not isinstance(p, int) or m >= 2:
                    dve.wait_ge(v_lo_kept, m - 1)
                for h in range(2):
                    ins = nc.vector.tensor_tensor(v_sum[:, par, h * D:(h + 1) * D],
                                                  psum[:, bank + WV, h * D:(h + 1) * D],
                                                  b_row[:, 2 * layer], ALU.add)
                ins.then_inc(v_summed, 1)
                if layer == 0:
                    dve.wait_ge(r_made, m + 1)
                    for h in range(2):
                        ins = nc.vector.tensor_tensor(x1[:, bass.ds(p * (2 * D) + h * D, D)],
                                                      psum[:, bank + WRES, h * D:(h + 1) * D],
                                                      b_row[:, 1], ALU.add)
                    ins.then_inc(r_kept, 1)

            def projections(layer):
                split_x(layer, 0, 0)
                split_x(layer, 1, 1)
                keep_projections(layer, 0, 0)
                split_x(layer, 2, 0)
                keep_projections(layer, 1, 1)
                split_x(layer, 3, 1)
                keep_projections(layer, 2, 0)
                with dve.Fori(2, PAIRS // 2) as i:
                    split_x(layer, i * 2, 0)
                    keep_projections(layer, i * 2 - 1, 1)
                    split_x(layer, i * 2 + 1, 1)
                    keep_projections(layer, i * 2, 0)
                keep_projections(layer, PAIRS - 1, 1)

            def split_q(layer, t, par):
                n = t + layer * TILES
                dve.wait_ge(q_hi_ready, n + 1)
                nc.vector.tensor_tensor(q_hl[:, par, 1], q_all[:, :, bass.ds(t * P, P)],
                                        q_hl[:, par, 0].bitcast(F32), ALU.subtract).then_inc(q_lo_ready, 1)

            def max_chunk(n, par, j):
                dve.wait_ge(scored, n * ROUNDS + (j + 1))
                nc.vector.reduce_max(chunk_max[:, par, j:j + 1], scores_ps[:, j, :], AX.X)\
                    .then_inc(chunk_maxed, 1)

            def invert(n, par):
                dve.wait_ge(exped, n + 1)
                nc.vector.reciprocal(inv_sum[:, par:par + 1], row_sum[:, par:par + 1]).then_inc(inverted, 1)

            def combine(n, par, j):
                if j == 0:
                    dve.wait_ge(inverted, n + 1)
                    if isinstance(n, int):
                        dve.wait_ge(adj_loaded[par], DMA * (n // 2 + 1))
                    else:
                        dve.wait_ge(adj_loaded[par], (n + (2 - par)) * (DMA // 2))
                at = slice(j * BANK, (j + 1) * BANK)
                nc.vector.scalar_tensor_tensor(probs[:, par, at], probs[:, par, at], inv_sum[:, par:par + 1],
                                               adj_sb[:, par, at], ALU.mult, ALU.add).then_inc(combined, 1)

            def mix_lo_round(n, par, j):
                dve.wait_ge(mix_hi, n * ROUNDS + (j + 1))
                nc.vector.tensor_tensor(mixT[:, par, 1, BLOCKS * j:BLOCKS * (j + 1), :],
                                        turned_ps[:, j % 2, :].rearrange("p (k a) -> p k a", a=P),
                                        mixT[:, par, 0, BLOCKS * j:BLOCKS * (j + 1), :].bitcast(F32),
                                        ALU.subtract).then_inc(mix_lo, 1)

            def add_residual(layer, t, par):
                n = t + layer * TILES
                dve.wait_ge(mixed, n + 1)
                if layer == 0 and (not isinstance(t, int) or t >= 2):
                    dve.wait_ge(x1_kept, t - 1)
                    dve.wait_ge(x1_turned, t - 1)
                if layer == 1 and (not isinstance(t, int) or t >= 2):
                    dve.wait_ge(normed, t - 1)
                nc.vector.scalar_tensor_tensor(y[:, par], mixed_ps, 0.0, x1[:, bass.ds(t * D, D)],
                                               ALU.max, ALU.add).then_inc(y_ready, 1)

            def statistics(t, par):
                dve.wait_ge(x_added, t + 1)
                nc.vector.bn_stats(stats[:, par], y[:, par]).then_inc(stats_made, 1)

            def moments(t, par):
                nc.vector.bn_aggr(mean_var[:, par], stats[:, par]).then_inc(moments_made, 1)

            def normalize(t, par):
                dve.wait_ge(std_made, t + 1)
                if isinstance(t, int):
                    if t >= 2:
                        dve.wait_ge(stored[par], DMA * (t // 2))
                else:
                    dve.wait_ge(stored[par], (t - par) * (DMA // 2))
                nc.vector.tensor_scalar(y_norm[:, par], y[:, par], mean_var[:, par, 0:1],
                                        inv_std[:, par:par + 1], ALU.subtract, ALU.mult).then_inc(normed, 1)

            def step(layer, t, par, on):
                n = t + layer * TILES
                for j in range(ROUNDS):
                    if on["previous"] and j < 2:
                        combine(n - 1, 1 - par, 2 + j)
                    if on["third"] and j == 2:
                        add_residual(layer, t - 3, 1 - par)
                    if on["tile"]:
                        max_chunk(n, par, j)
                if on["tile"]:
                    dve.wait_ge(chunk_maxed, (n + 1) * ROUNDS)
                    nc.vector.tensor_reduce(neg_max[:, par:par + 1], chunk_max[:, par], AX.X, ALU.max,
                                            negate=True).then_inc(maxed, 1)
                if on["previous"]:
                    mix_lo_round(n - 1, 1 - par, 0)
                if layer == 1 and on["third"]:
                    statistics(t - 3, 1 - par)
                    dve.wait_ge(stats_made, t - 2)
                if on["previous"]:
                    mix_lo_round(n - 1, 1 - par, 1)
                if layer == 1 and on["third"]:
                    moments(t - 3, 1 - par)
                if on["next"]:
                    split_q(layer, t + 1, 1 - par)
                if on["tile"]:
                    invert(n, par)
                    combine(n, par, 0)
                if on["previous"]:
                    mix_lo_round(n - 1, 1 - par, 2)
                if on["tile"]:
                    combine(n, par, 1)
                if on["previous"]:
                    mix_lo_round(n - 1, 1 - par, 3)
                if layer == 1 and on["third"]:
                    normalize(t - 3, 1 - par)

            split_weights(0, 4)
            for layer in range(LAYERS):
                if layer == 1:
                    dve.wait_ge(turned, ROUNDS * TILES)
                projections(layer)
                split_q(layer, 0, 0)
                if layer == 0:
                    split_weights(1, 3)
                over_steps(dve, lambda t, par, on, layer=layer: step(layer, t, par, on))

        @block.tensor
        def _(pe):
            def projections(layer, p, par):
                m = p + layer * PAIRS
                bank = 4 * par
                pe.wait_ge(x_lo_done, m + 1)
                def feature_major(w, made):
                    for cc in range(CC):
                        for i, (a, b) in enumerate((a, b) for a, b in PARTS):
                            for dc in range(CC):
                                ins = nc.tensor.matmul(psum[:, bank + w, cc * PAIR:(cc + 1) * PAIR],
                                                       w_hl[:, a, w, dc, cc * P:(cc + 1) * P],
                                                       x_hl[:, par, b, dc, :],
                                                       start=(i == 0 and dc == 0), stop=(i == 2 and dc == CC - 1))
                    ins.then_inc(made, 1)

                def row_major(w, made):
                    for h in range(2):
                        for i, (a, b) in enumerate(PARTS):
                            for dc in range(CC):
                                ins = nc.tensor.matmul(psum[:, bank + w, h * D:(h + 1) * D],
                                                       x_hl[:, par, a, dc, h * P:(h + 1) * P],
                                                       w_hl[:, b, w, dc, :],
                                                       start=(i == 0 and dc == 0), stop=(i == 2 and dc == CC - 1))
                    ins.then_inc(made, 1)

                looped = not isinstance(p, int)
                if looped:
                    pe.wait_ge(k_lo_kept, m - 1)
                feature_major(WK, k_made)
                if looped:
                    pe.wait_ge(q_kept, m - 1)
                feature_major(WQ, q_made)
                if looped:
                    pe.wait_ge(v_summed, m - 1)
                row_major(WV, v_made)
                if layer == 0:
                    if looped:
                        pe.wait_ge(r_kept, m - 1)
                    row_major(WRES, r_made)

            def scores(layer, t, par):
                n = t + layer * TILES
                pe.wait_ge(q_lo_ready, n + 1)
                if isinstance(t, int) and t == 0:
                    pe.wait_ge(q_kept, PAIRS * (layer + 1))
                    pe.wait_ge(k_lo_kept, PAIRS * (layer + 1))
                    pe.wait_ge(v_summed, PAIRS * (layer + 1))
                    pe.wait_ge(r_kept, PAIRS)
                else:
                    pe.wait_ge(exped, n)
                for j in range(ROUNDS):
                    for i, (a, b) in enumerate(PARTS):
                        for cc in range(CC):
                            ins = nc.tensor.matmul(scores_ps[:, j, :], q_hl[:, par, a, cc, :],
                                                   k_hl[:, b, cc, j * BANK:(j + 1) * BANK],
                                                   start=(i == 0 and cc == 0), stop=(i == 2 and cc == CC - 1))
                    ins.then_inc(scored, 1)

            def turn_round(n, par, j):
                pe.wait_ge(combined, n * ROUNDS + (j + 1))
                if not isinstance(n, int) or n * ROUNDS + j >= 2:
                    pe.wait_ge(mix_lo, n * ROUNDS + (j - 1))
                for k in range(BLOCKS):
                    at = (BLOCKS * j + k) * P
                    ins = nc.tensor.transpose(turned_ps[:, j % 2, k * P:(k + 1) * P],
                                              probs[:, par, at:at + P], ident[:])
                ins.then_inc(turned, 1)

            def mix_round(n, par, j):
                pe.wait_ge(mix_lo, n * ROUNDS + (j + 1))
                if j == 0 and (not isinstance(n, int) or n >= 1):
                    pe.wait_ge(y_ready, n)
                for bt in range(BLOCKS * j, BLOCKS * (j + 1)):
                    for i, (a, b) in enumerate(PARTS):
                        ins = nc.tensor.matmul(mixed_ps, mixT[:, par, a, bt, :],
                                               v_hl[:, b, bt * D:(bt + 1) * D],
                                               start=(bt == 0 and i == 0), stop=(bt == TILES - 1 and i == 2))
                if j == ROUNDS - 1:
                    ins.then_inc(mixed, 1)

            def turn_x1(t, par):
                pe.wait_ge(y_ready, t + 1)
                if not isinstance(t, int) or t >= 1:
                    pe.wait_ge(x1T_kept, t)
                for cc in range(CC):
                    ins = nc.tensor.transpose(x1T_ps[:, cc * P:(cc + 1) * P],
                                              y[:, par, cc * P:(cc + 1) * P], ident[:])
                ins.then_inc(x1_turned, 1)

            def step(layer, t, par, on):
                n = t + layer * TILES
                if on["tile"]:
                    scores(layer, t, par)
                if layer == 0 and on["third"]:
                    turn_x1(t - 3, 1 - par)
                for j in range(ROUNDS):
                    if on["previous"]:
                        turn_round(n - 1, 1 - par, j)
                    if on["second"]:
                        mix_round(n - 2, par, j)

            pe.wait_ge(w_lo_done, 4)
            for layer in range(LAYERS):
                if layer == 1:
                    pe.wait_ge(exped, TILES)
                    pe.wait_ge(mix_lo, TILES * ROUNDS)
                    pe.wait_ge(y_ready, TILES)
                    pe.wait_ge(w_lo_done, 7)
                projections(layer, 0, 0)
                projections(layer, 1, 1)
                with pe.Fori(1, PAIRS // 2) as i:
                    for par in range(2):
                        projections(layer, i * 2 + par, par)
                if layer == 0:
                    pe.wait_ge(b_loaded, 5 * DMA)
                over_steps(pe, lambda t, par, on, layer=layer: step(layer, t, par, on))


def kernel(**inputs):
    import numpy as np
    import concourse.bacc as bacc
    from concourse.bass_utils import run_bass_kernel_spmd

    nc = bacc.Bacc("TRN2", target_bir_lowering=False, num_devices=1)
    arrays = {}

    def dram(name, a):
        a = np.ascontiguousarray(a)
        arrays[name] = a
        return nc.dram_tensor(name, a.shape, mybir.dt.from_np(a.dtype), kind="ExternalInput").ap()

    w = {k[len("L0_gnn_"):]: np.asarray(v) for k, v in inputs.items() if k.startswith("L0_gnn_")}
    x = np.asarray(inputs["x"])
    x_ap = dram("x_rows", x)
    xT_ap = dram("x_columns", x.T)
    adj_ap = dram("adj", np.asarray(inputs["adj"]))
    weights = [[dram(f"{name}T", w[name].T) for name in names]
               for names in (("wq0", "wk0", "wv0", "wres"), ("wq1", "wk1", "wv1"))]
    cols = dram("bias_columns", np.stack([[w[f"b{n}{layer}"].reshape(D // P, P) for n in "qk"]
                                          for layer in range(LAYERS)]).transpose(3, 0, 1, 2))
    rows = [dram(name, w[name]) for name in ("bv0", "bres", "bv1")]
    ident = dram("identity", np.eye(P, dtype=np.float32))
    out = nc.dram_tensor("out", (N, D), F32, kind="ExternalOutput").ap()
    two_layer_attention(nc, x_ap, xT_ap, adj_ap, weights, cols, rows, ident, out)
    return run_bass_kernel_spmd(nc, [arrays], core_ids=[0]).results[0]["out"]
```

```python
from contextlib import ExitStack

import concourse.bass as bass
from concourse import mybir
from concourse.alu_op_type import AluOpType as ALU

F32 = mybir.dt.float32
F32R = mybir.dt.float32r
ACT = mybir.ActivationFunctionType
AX = mybir.AxisListType

P = 128
N = 2048
D = 256
CC = D // P
TILES = N // P
PAIRS = TILES // 2
PAIR = 2 * P
BANK = 512
ROUNDS = N // BANK
BLOCKS = BANK // P
LAYERS = 2
DMA = 16
EPS = 1e-5
Q_SCALE = D ** -0.5
NEXT_WEIGHTS = {3: 0, 4: 1, 5: 2}
NEXT_EARLY = {TILES: (0, 1), TILES + 1: (2,), TILES + 2: (3, 4, 5, 6, 7)}
LATE = ((0, 1), (2, 3, 4), (5, 6, 7))
LATE_X = [{p: (p,) for p in range(8)}, {2: (0,), 3: (1,), 4: (2,), 5: (3,), 6: (4, 5), 7: (6, 7)}]
PARTS = ((0, 0), (1, 0), (0, 1))
WK, WQ, WV, WRES = range(4)


def two_layer_attention(nc, x, xT, adj, weights, cols, rows, ident_in, out):
    with ExitStack() as ctx:
        def sb(name, shape, dt=F32):
            return ctx.enter_context(nc.sbuf_tensor(name, shape, dt))

        def sem(name):
            return ctx.enter_context(nc.semaphore(name))

        x_t = sb("x_t", [P, CC, N])
        q_all = sb("q_all", [P, CC, N])
        k_hl = sb("k_hl", [P, 2, CC, N], F32R)
        v_hl = sb("v_hl", [P, 2, TILES * D], F32R)
        x1 = sb("x1", [P, TILES * D])
        w_hl = sb("w_hl", [P, 2, 4, CC, D], F32R)
        mixT = sb("mixT", [P, 2, 2, TILES, P], F32R)
        x_hl = sb("x_hl", [P, 2, 2, CC, PAIR], F32R)
        probs = sb("probs", [P, N])
        mix = sb("mix", [P, 2, N])
        ident = sb("ident", [P, P])
        q_hl = sb("q_hl", [P, 2, 2, CC, P], F32R)
        x_row = sb("x_row", [P, 2, D])
        y = sb("y", [P, 2, D])
        y_norm = sb("y_norm", [P, 2, D])
        b_col = sb("b_col", [P, LAYERS, 2, CC])
        bq_scaled = sb("bq_scaled", [P, LAYERS, CC])
        b_row = sb("b_row", [P, 3, D])
        chunk_max = sb("chunk_max", [P, 2, ROUNDS])
        neg_max = sb("neg_max", [P, 2])
        row_sum = sb("row_sum", [P, 2])
        inv_sum = sb("inv_sum", [P, 2])
        stats = sb("stats", [P, 2, 6])
        mean_var = sb("mean_var", [P, 2, 2])
        var_eps = sb("var_eps", [P, 2])
        inv_std = sb("inv_std", [P, 2])
        minus_half = sb("minus_half", [P, 1])
        eps = sb("eps", [P, 1])

        v_sum = [y, y_norm, x_row]
        late_x = mixT.rearrange("p s h t a -> p (s h t a)").rearrange("p (h c n) -> p h c n", h=2, c=CC)
        w_raw = [[mix[:, 1, w * CC * D:(w + 1) * CC * D].rearrange("p (c n) -> p c n", c=CC) for w in range(4)],
                 [x_row[:], y_norm[:], x_row[:]]]

        psum = ctx.enter_context(nc.psum_tensor("psum", [P, 8, BANK], F32))
        scores_ps = psum[:, 0:ROUNDS, :]
        turned_ps = psum[:, ROUNDS:ROUNDS + 2, :]
        mixed_ps = psum[:, 6, 0:D]
        x1T_ps = psum[:, 7, 0:D]

        def early_ps(which, par):
            return psum[:, 2 * par + which, :]

        def late_ps(which, par):
            return psum[:, 4 + 2 * par + which, :]

        w_loaded = [sem(f"w_loaded{i}") for i in range(4)]
        b_loaded = sem("b_loaded")
        w_hi_done, w_lo_done = sem("w_hi_done"), sem("w_lo_done")
        bq_done = sem("bq_done")
        x_loaded = [sem(f"x_loaded{i}") for i in range(2)]
        x_hi_done, x_lo_done = sem("x_hi_done"), sem("x_lo_done")
        late_hi_done, late_lo_done = sem("late_hi_done"), sem("late_lo_done")
        q_made, k_made, v_made, r_made = (sem(f"{n}_made") for n in "qkvr")
        q_kept, k_hi_kept = sem("q_kept"), sem("k_hi_kept")
        k_lo_kept, v_summed, r_kept = sem("k_lo_kept"), sem("v_summed"), sem("r_kept")
        v_hi_kept, v_lo_kept = sem("v_hi_kept"), sem("v_lo_kept")
        q_hi_ready, q_lo_ready = sem("q_hi_ready"), sem("q_lo_ready")
        scored = sem("scored")
        chunk_maxed, maxed = sem("chunk_maxed"), sem("maxed")
        exped = sem("exped")
        inverted = sem("inverted")
        adj_loaded = [sem(f"adj_loaded{i}") for i in range(2)]
        combined = sem("combined")
        turned = sem("turned")
        mix_hi, mix_lo = sem("mix_hi"), sem("mix_lo")
        mixed = sem("mixed")
        y_ready = sem("y_ready")
        x1_kept = sem("x1_kept")
        x1_turned = sem("x1_turned")
        x1T_kept = sem("x1T_kept")
        row_loaded = [sem(f"row_loaded{i}") for i in range(2)]
        x_added = sem("x_added")
        stats_made, moments_made = sem("stats_made"), sem("moments_made")
        eps_added, std_made = sem("eps_added"), sem("std_made")
        consts_made = sem("consts_made")
        normed = sem("normed")
        stored = [sem(f"stored{i}") for i in range(2)]

        block = ctx.enter_context(nc.Block())

        def on(t):
            return {"tile": t < TILES, "previous": 1 <= t <= TILES,
                    "second": 2 <= t <= TILES + 1, "third": 3 <= t <= TILES + 2,
                    "next": 1 <= t < TILES - 1}

        def over_steps(eng, step):
            for t in range(6):
                step(t, t % 2, on(t))
            with eng.Fori(3, TILES // 2 - 1) as i:
                for par in range(2):
                    step(i * 2 + par, par, on(6))
            for t in range(TILES - 2, TILES + 3):
                step(t, t % 2, on(t))

        @block.sync
        def _(sp):
            xT_v = xT.rearrange("(c p) n -> p c n", p=P)

            def load_weight(layer, w):
                sp.dma_start(w_raw[layer][w], weights[layer][w].rearrange("(c p) n -> p c n", p=P))\
                    .then_inc(w_loaded[w], DMA)

            def load_adj(layer, t):
                if layer == 1:
                    sp.wait_ge(turned, (TILES + t - 1) * ROUNDS)
                elif t == 1:
                    sp.wait_ge(w_lo_done, 4)
                sp.dma_start(mix[:, t], adj[t * P:(t + 1) * P, :]).then_inc(adj_loaded[t], DMA)

            load_weight(0, WK)
            sp.dma_start(x_t[:, :, 0:PAIR], xT_v[:, :, 0:PAIR]).then_inc(x_loaded[0], DMA)
            load_weight(0, WQ)
            sp.dma_start(x_t[:, :, PAIR:2 * PAIR], xT_v[:, :, PAIR:2 * PAIR]).then_inc(x_loaded[1], DMA)
            load_weight(0, WV)
            load_weight(0, WRES)
            with sp.Fori(1, PAIRS // 2) as i:
                for par in range(2):
                    columns = bass.ds((i * 2 + par) * PAIR, PAIR)
                    sp.wait_ge(x_loaded[par], i * DMA)
                    sp.dma_start(x_t[:, :, columns], xT_v[:, :, columns]).then_inc(x_loaded[par], DMA)
            for layer in range(LAYERS):
                load_adj(layer, 0)
                load_adj(layer, 1)
                with sp.Fori(1, TILES // 2) as i:
                    for par in range(2):
                        t = i * 2 + par
                        sp.wait_ge(turned, (t + (layer * TILES - 1)) * ROUNDS)
                        sp.dma_start(mix[:, par], adj[bass.ds(t * P, P), :])\
                            .then_inc(adj_loaded[par], DMA)

        @block.gpsimd
        def _(pool):
            pool.dma_start(b_col[:], cols).then_inc(b_loaded, DMA)
            for i, b in enumerate(rows):
                pool.dma_start(b_row[:, i], b.partition_broadcast(P)).then_inc(b_loaded, DMA)
            pool.dma_start(ident[:], ident_in).then_inc(b_loaded, DMA)
            pool.memset(minus_half[:], -0.5).then_inc(consts_made, 1)
            pool.memset(eps[:], EPS).then_inc(consts_made, 1)

            def keep_v_lo(layer):
                for p in range(PAIRS):
                    pool.wait_ge(v_hi_kept, layer * PAIRS + p + 1)
                    at = slice(p * 2 * D, (p + 1) * 2 * D)
                    pool.tensor_tensor(v_hl[:, 1, at], v_sum[p % 3].rearrange("p h c -> p (h c)"),
                                       v_hl[:, 0, at].bitcast(F32), ALU.subtract).then_inc(v_lo_kept, 1)

            def keep_x1(t, par):
                pool.wait_ge(y_ready, t + 1)
                pool.tensor_copy(x1[:, bass.ds(t * D, D)], y[:, par]).then_inc(x1_kept, 1)

            def norm_step(t, par):
                pool.wait_ge(row_loaded[par], (t + (2 - par)) * (DMA // 2))
                pool.tensor_tensor(x_row[:, par], x_row[:, par], x1[:, bass.ds(t * D, D)], ALU.add)\
                    .then_inc(x_added, 1)
                pool.wait_ge(moments_made, t + 1)
                pool.tensor_tensor(var_eps[:, par:par + 1], mean_var[:, par, 1:2], eps[:], ALU.add)\
                    .then_inc(eps_added, 1)
                pool.wait_ge(eps_added, t + 1)
                pool.tensor_tensor(inv_std[:, par:par + 1], var_eps[:, par:par + 1], minus_half[:],
                                   ALU.pow).then_inc(std_made, 1)

            keep_v_lo(0)
            with pool.Fori(0, TILES // 2) as i:
                for par in range(2):
                    keep_x1(i * 2 + par, par)
            keep_v_lo(1)
            pool.wait_ge(consts_made, 2)
            with pool.Fori(0, TILES // 2) as i:
                for par in range(2):
                    norm_step(i * 2 + par, par)

        @block.scalar
        def _(act):
            def load_next_weight(w):
                if w in (WK, WQ):
                    act.wait_ge(v_lo_kept, PAIRS)
                if w == WV:
                    act.wait_ge(w_lo_done, 4 + WK + 1)
                act.dma_start(w_raw[1][w], weights[1][w].rearrange("(c p) n -> p c n", p=P))\
                    .then_inc(w_loaded[w], DMA)

            def split_weight(layer, w):
                act.wait_ge(w_loaded[w], DMA * (layer + 1))
                nc.scalar.activation(w_hl[:, 0, w], w_raw[layer][w], ACT.Copy).then_inc(w_hi_done, 1)

            def split_x(layer, p):
                if p >= 2:
                    act.wait_ge(q_made, layer * PAIRS + p - 1)
                if layer == 0:
                    act.wait_ge(x_loaded[p % 2], (p // 2 + 1) * DMA)
                else:
                    act.wait_ge(x1T_kept, 2 * p + 2)
                nc.scalar.activation(x_hl[:, p % 2, 0], x_t[:, :, p * PAIR:(p + 1) * PAIR], ACT.Copy)\
                    .then_inc(x_hi_done, 1)

            def split_late_x(layer, p):
                at = slice(p * PAIR, (p + 1) * PAIR)
                if layer == 0:
                    act.wait_ge(x_loaded[p % 2], (p // 2 + 1) * DMA)
                else:
                    act.wait_ge(x1T_kept, 2 * p + 2)
                    act.wait_ge(mixed, TILES)
                nc.scalar.activation(late_x[:, 0, :, at], x_t[:, :, at], ACT.Copy).then_inc(late_hi_done, 1)

            def keep_early(layer, p):
                m = layer * PAIRS + p
                at = slice(p * PAIR, (p + 1) * PAIR)
                act.wait_ge(k_made, m + 1)
                for cc in range(CC):
                    ins = nc.scalar.activation(k_hl[:, 0, cc, at], early_ps(WK, p % 2)[:, cc * PAIR:(cc + 1) * PAIR],
                                               ACT.Identity, bias=b_col[:, layer, 1, cc:cc + 1])
                ins.then_inc(k_hi_kept, 1)
                act.wait_ge(q_made, m + 1)
                for cc in range(CC):
                    ins = nc.scalar.activation(q_all[:, cc, at], early_ps(WQ, p % 2)[:, cc * PAIR:(cc + 1) * PAIR],
                                               ACT.Identity, bias=bq_scaled[:, layer, cc:cc + 1], scale=Q_SCALE)
                ins.then_inc(q_kept, 1)

            def keep_late(layer, p):
                act.wait_ge(v_summed, layer * PAIRS + p + 1)
                nc.scalar.activation(v_hl[:, 0, p * 2 * D:(p + 1) * 2 * D],
                                     v_sum[p % 3].rearrange("p h c -> p (h c)"), ACT.Copy)\
                    .then_inc(v_hi_kept, 1)

            def split_q(layer, t, par):
                n = t + layer * TILES
                if not isinstance(t, int) or n >= 2:
                    act.wait_ge(scored, (n - 1) * ROUNDS)
                nc.scalar.activation(q_hl[:, par, 0], q_all[:, :, bass.ds(t * P, P)], ACT.Copy)\
                    .then_inc(q_hi_ready, 1)

            def mix_hi_round(layer, t, par, j):
                n = t + layer * TILES
                act.wait_ge(turned, n * ROUNDS + (j + 1))
                if not isinstance(t, int) or n >= 2:
                    if j == 0:
                        act.wait_ge(mixed, n - 1)
                nc.scalar.activation(mixT[:, par, 0, BLOCKS * j:BLOCKS * (j + 1), :],
                                     turned_ps[:, j % 2, :].rearrange("p (k a) -> p k a", a=P),
                                     ACT.Copy).then_inc(mix_hi, 1)

            def step(layer, t, par, on):
                n = t + layer * TILES
                if layer == 1 and (not isinstance(t, int) or t >= 4):
                    store(t - 4, par)
                first = isinstance(t, int) and t < 2
                if first and on["next"]:
                    split_q(layer, t + 1, 1 - par)
                if isinstance(t, int) and t == 2:
                    if layer == 1:
                        act.wait_ge(v_lo_kept, LAYERS * PAIRS)
                        load_row(0, 0)
                    for j in range(ROUNDS):
                        mix_hi_round(layer, 0, 0, j)
                if layer == 0 and isinstance(t, int) and t == 2:
                    load_next_weight(WK)
                    load_next_weight(WQ)
                if layer == 0 and isinstance(t, int) and t == 4:
                    load_next_weight(WV)
                if on["previous"] and not first:
                    mix_hi_round(layer, t - 1, 1 - par, 0)
                if on["tile"]:
                    act.wait_ge(maxed, n + 1)
                    if not isinstance(t, int) or n >= 1:
                        act.wait_ge(combined, n * ROUNDS)
                    nc.scalar.activation(probs[:], scores_ps.rearrange("p j n -> p (j n)"), ACT.Exp,
                                         bias=neg_max[:, par:par + 1], scale=1.0,
                                         accum_out=row_sum[:, par:par + 1]).then_inc(exped, 1)
                if first:
                    for p in LATE[t + 1]:
                        keep_late(layer, p)
                if on["next"] and not first:
                    split_q(layer, t + 1, 1 - par)
                if on["previous"] and not first:
                    mix_hi_round(layer, t - 1, 1 - par, 1)
                if layer == 0 and isinstance(t, int) and t == TILES + 2:
                    early(1, (3,))
                if layer == 0 and on["third"]:
                    act.wait_ge(x1_turned, t - 2)
                    nc.scalar.activation(x_t[:, :, bass.ds((t - 3) * P, P)],
                                         x1T_ps.rearrange("p (c a) -> p c a", c=CC), ACT.Copy)\
                        .then_inc(x1T_kept, 1)
                if on["previous"] and not first:
                    mix_hi_round(layer, t - 1, 1 - par, 2)
                    mix_hi_round(layer, t - 1, 1 - par, 3)
                    if layer == 1:
                        load_row(t - 1, 1 - par)
                if layer == 0 and isinstance(t, int) and t in NEXT_WEIGHTS:
                    split_weight(1, NEXT_WEIGHTS[t])
                if layer == 0 and isinstance(t, int) and t == TILES - 2:
                    split_x(1, 0)
                    split_x(1, 1)
                if layer == 0 and isinstance(t, int) and t in NEXT_EARLY:
                    early(1, [p for p in NEXT_EARLY[t] if p != 3])

            def load_row(t, par):
                if not isinstance(t, int) or t >= 2:
                    act.wait_ge(y_ready, t + (TILES - 1))
                act.dma_start(x_row[:, par], x[bass.ds(t * P, P), :]).then_inc(row_loaded[par], DMA)

            def store(t, par):
                act.wait_ge(normed, t + 1)
                act.dma_start(out[bass.ds(t * P, P), :], y_norm[:, par]).then_inc(stored[par], DMA)

            def early(layer, pairs):
                for p in pairs:
                    if p == 0 and layer == 0:
                        split_x(layer, 0)
                        split_weight(0, WQ)
                        split_x(layer, 1)
                        split_weight(0, WV)
                        split_weight(0, WRES)
                        act.wait_ge(b_loaded, 5 * DMA)
                        act.wait_ge(bq_done, 1)
                    if p == PAIRS - 1:
                        split_q(layer, 0, 0)
                        split_q(layer, 1, 1)
                    keep_early(layer, p)
                    if p + 2 < PAIRS:
                        split_x(layer, p + 2)
                    for late in LATE_X[layer].get(p, ()):
                        split_late_x(layer, late)

            split_weight(0, WK)
            early(0, range(PAIRS))
            for layer in range(LAYERS):
                for p in LATE[0]:
                    keep_late(layer, p)
                over_steps(act, lambda t, par, on, layer=layer: step(layer, t, par, on))
            for t in range(TILES - 1, TILES):
                store(t, t % 2)
            for par in range(2):
                act.wait_ge(stored[par], DMA * (TILES // 2))

        @block.vector
        def _(dve):
            def split_weight(layer, w):
                dve.wait_ge(w_hi_done, 4 * layer + w + 1)
                nc.vector.tensor_tensor(w_hl[:, 1, w], w_raw[layer][w], w_hl[:, 0, w].bitcast(F32),
                                        ALU.subtract).then_inc(w_lo_done, 1)

            def split_x(layer, p):
                dve.wait_ge(x_hi_done, layer * PAIRS + p + 1)
                nc.vector.tensor_tensor(x_hl[:, p % 2, 1], x_t[:, :, p * PAIR:(p + 1) * PAIR],
                                        x_hl[:, p % 2, 0].bitcast(F32), ALU.subtract).then_inc(x_lo_done, 1)

            def split_late_x(layer, p):
                at = slice(p * PAIR, (p + 1) * PAIR)
                dve.wait_ge(late_hi_done, layer * PAIRS + p + 1)
                nc.vector.tensor_tensor(late_x[:, 1, :, at], x_t[:, :, at], late_x[:, 0, :, at].bitcast(F32),
                                        ALU.subtract).then_inc(late_lo_done, 1)

            def keep_early(layer, p):
                at = slice(p * PAIR, (p + 1) * PAIR)
                dve.wait_ge(k_hi_kept, layer * PAIRS + p + 1)
                for cc in range(CC):
                    ins = nc.vector.scalar_tensor_tensor(
                        k_hl[:, 1, cc, at], early_ps(WK, p % 2)[:, cc * PAIR:(cc + 1) * PAIR],
                        b_col[:, layer, 1, cc:cc + 1], k_hl[:, 0, cc, at].bitcast(F32),
                        ALU.add, ALU.subtract)
                ins.then_inc(k_lo_kept, 1)

            def keep_late(layer, p):
                m = layer * PAIRS + p
                dve.wait_ge(v_made, m + 1)
                if p >= 3:
                    dve.wait_ge(v_lo_kept, m - 2)
                if layer == 1 and p == 0:
                    dve.wait_ge(x1_kept, TILES)
                for h in range(2):
                    ins = nc.vector.tensor_tensor(v_sum[p % 3][:, h], late_ps(1, p % 2)[:, h * D:(h + 1) * D],
                                                  b_row[:, 2 * layer], ALU.add)
                ins.then_inc(v_summed, 1)
                if layer == 0:
                    for h in range(2):
                        ins = nc.vector.tensor_tensor(x1[:, (2 * p + h) * D:(2 * p + h + 1) * D],
                                                      late_ps(0, p % 2)[:, h * D:(h + 1) * D],
                                                      b_row[:, 1], ALU.add)
                    ins.then_inc(r_kept, 1)

            def early(layer, pairs):
                for p in pairs:
                    if p == 0 and layer == 0:
                        split_x(layer, 0)
                        split_weight(0, WQ)
                        split_x(layer, 1)
                        split_weight(0, WV)
                        split_weight(0, WRES)
                        dve.wait_ge(b_loaded, 5 * DMA)
                        nc.vector.tensor_scalar(bq_scaled[:], b_col[:, :, 0, :], Q_SCALE, None, ALU.mult)\
                            .then_inc(bq_done, 1)
                    if p == PAIRS - 1:
                        split_q(layer, 0, 0)
                        split_q(layer, 1, 1)
                    keep_early(layer, p)
                    if p + 2 < PAIRS:
                        split_x(layer, p + 2)
                    for late in LATE_X[layer].get(p, ()):
                        split_late_x(layer, late)

            def split_q(layer, t, par):
                n = t + layer * TILES
                dve.wait_ge(q_hi_ready, n + 1)
                nc.vector.tensor_tensor(q_hl[:, par, 1], q_all[:, :, bass.ds(t * P, P)],
                                        q_hl[:, par, 0].bitcast(F32), ALU.subtract).then_inc(q_lo_ready, 1)

            def max_chunk(n, par, j):
                dve.wait_ge(scored, n * ROUNDS + (j + 1))
                nc.vector.reduce_max(chunk_max[:, par, j:j + 1], scores_ps[:, j, :], AX.X)\
                    .then_inc(chunk_maxed, 1)

            def invert(n, par):
                dve.wait_ge(exped, n + 1)
                nc.vector.reciprocal(inv_sum[:, par:par + 1], row_sum[:, par:par + 1]).then_inc(inverted, 1)

            def combine(n, par, j):
                if j == 0:
                    dve.wait_ge(inverted, n + 1)
                    if isinstance(n, int):
                        dve.wait_ge(adj_loaded[par], DMA * (n // 2 + 1))
                    else:
                        dve.wait_ge(adj_loaded[par], (n + (2 - par)) * (DMA // 2))
                at = slice(j * BANK, (j + 1) * BANK)
                nc.vector.scalar_tensor_tensor(mix[:, par, at], probs[:, at], inv_sum[:, par:par + 1],
                                               mix[:, par, at], ALU.mult, ALU.add).then_inc(combined, 1)

            def mix_lo_round(n, par, j):
                dve.wait_ge(mix_hi, n * ROUNDS + (j + 1))
                nc.vector.tensor_tensor(mixT[:, par, 1, BLOCKS * j:BLOCKS * (j + 1), :],
                                        turned_ps[:, j % 2, :].rearrange("p (k a) -> p k a", a=P),
                                        mixT[:, par, 0, BLOCKS * j:BLOCKS * (j + 1), :].bitcast(F32),
                                        ALU.subtract).then_inc(mix_lo, 1)

            def add_residual(layer, t, par):
                n = t + layer * TILES
                dve.wait_ge(mixed, n + 1)
                if layer == 0 and (not isinstance(t, int) or t >= 2):
                    dve.wait_ge(x1_kept, t - 1)
                    dve.wait_ge(x1_turned, t - 1)
                if layer == 1 and (not isinstance(t, int) or t >= 2):
                    dve.wait_ge(normed, t - 1)
                if layer == 1:
                    dve.wait_ge(x_added, t + 1)
                residual = x_row[:, par] if layer else x1[:, bass.ds(t * D, D)]
                nc.vector.scalar_tensor_tensor(y[:, par], mixed_ps, 0.0, residual, ALU.max, ALU.add)\
                    .then_inc(y_ready, 1)

            def statistics(t, par):
                dve.wait_ge(y_ready, t + (TILES + 1))
                nc.vector.bn_stats(stats[:, par], y[:, par]).then_inc(stats_made, 1)

            def moments(t, par):
                nc.vector.bn_aggr(mean_var[:, par], stats[:, par]).then_inc(moments_made, 1)

            def normalize(t, par):
                dve.wait_ge(std_made, t + 1)
                if isinstance(t, int):
                    if t >= 2:
                        dve.wait_ge(stored[par], DMA * (t // 2))
                else:
                    dve.wait_ge(stored[par], (t - par) * (DMA // 2))
                nc.vector.tensor_scalar(y_norm[:, par], y[:, par], mean_var[:, par, 0:1],
                                        inv_std[:, par:par + 1], ALU.subtract, ALU.mult).then_inc(normed, 1)

            def step(layer, t, par, on):
                n = t + layer * TILES
                first = isinstance(t, int) and t < 2
                tail = isinstance(t, int) and t >= TILES
                if tail and t == TILES:
                    add_residual(layer, t - 3, 1 - par)
                for j in range(ROUNDS):
                    if on["previous"] and j < 2:
                        combine(n - 1, 1 - par, 2 + j)
                    if on["third"] and not tail and j == 2:
                        add_residual(layer, t - 3, 1 - par)
                    if on["tile"]:
                        max_chunk(n, par, j)
                    if j == ROUNDS - 1 and on["tile"]:
                        dve.wait_ge(chunk_maxed, (n + 1) * ROUNDS)
                        nc.vector.tensor_reduce(neg_max[:, par:par + 1], chunk_max[:, par], AX.X, ALU.max,
                                                negate=True).then_inc(maxed, 1)
                    if isinstance(t, int) and t == 2:
                        mix_lo_round(n - 2, par, j)
                if first and on["next"]:
                    split_q(layer, t + 1, 1 - par)
                if first:
                    for p in LATE[t + 1]:
                        keep_late(layer, p)
                if on["previous"] and not first:
                    mix_lo_round(n - 1, 1 - par, 0)
                if layer == 1 and on["third"]:
                    statistics(t - 3, 1 - par)
                    dve.wait_ge(stats_made, t - 2)
                if on["previous"] and not first:
                    mix_lo_round(n - 1, 1 - par, 1)
                if layer == 1 and on["third"]:
                    moments(t - 3, 1 - par)
                if on["next"] and not first:
                    split_q(layer, t + 1, 1 - par)
                if on["tile"]:
                    invert(n, par)
                    combine(n, par, 0)
                if on["previous"] and not first:
                    mix_lo_round(n - 1, 1 - par, 2)
                if on["tile"]:
                    combine(n, par, 1)
                if on["previous"] and not first:
                    mix_lo_round(n - 1, 1 - par, 3)
                if layer == 1 and on["third"]:
                    normalize(t - 3, 1 - par)
                if tail and t < TILES + 2:
                    add_residual(layer, t - 2, par)
                if layer == 0 and isinstance(t, int) and t in NEXT_WEIGHTS:
                    split_weight(1, NEXT_WEIGHTS[t])
                if layer == 0 and isinstance(t, int) and t == TILES - 2:
                    split_x(1, 0)
                    split_x(1, 1)
                if layer == 0 and isinstance(t, int) and t in NEXT_EARLY:
                    early(1, NEXT_EARLY[t])

            split_weight(0, WK)
            early(0, range(PAIRS))
            for layer in range(LAYERS):
                for p in LATE[0]:
                    keep_late(layer, p)
                over_steps(dve, lambda t, par, on, layer=layer: step(layer, t, par, on))

        @block.tensor
        def _(pe):
            def feature_major(bank, w, par):
                for cc in range(CC):
                    for i, (a, b) in enumerate(PARTS):
                        for dc in range(CC):
                            ins = nc.tensor.matmul(bank[:, cc * PAIR:(cc + 1) * PAIR],
                                                   w_hl[:, a, w, dc, cc * P:(cc + 1) * P],
                                                   x_hl[:, par, b, dc, :],
                                                   start=(i == 0 and dc == 0), stop=(i == 2 and dc == CC - 1))
                return ins

            def row_major(bank, w, p):
                for h in range(2):
                    for i, (a, b) in enumerate(PARTS):
                        for dc in range(CC):
                            ins = nc.tensor.matmul(bank[:, h * D:(h + 1) * D],
                                                   late_x[:, a, dc, (2 * p + h) * P:(2 * p + h + 1) * P],
                                                   w_hl[:, b, w, dc, :],
                                                   start=(i == 0 and dc == 0), stop=(i == 2 and dc == CC - 1))
                return ins

            def make_early(layer, p, par):
                m = p + layer * PAIRS
                looped = not isinstance(p, int)
                pe.wait_ge(x_lo_done, m + 1)
                if looped or p >= 2:
                    pe.wait_ge(k_lo_kept, m - 1)
                feature_major(early_ps(WK, par), WK, par).then_inc(k_made, 1)
                if looped or p >= 2:
                    pe.wait_ge(q_kept, m - 1)
                if layer == 0 and not looped and p == 0:
                    pe.wait_ge(w_lo_done, 2)
                feature_major(early_ps(WQ, par), WQ, par).then_inc(q_made, 1)

            def make_late(layer, p):
                m = p + layer * PAIRS
                pe.wait_ge(late_lo_done, m + 1)
                if p >= 2:
                    pe.wait_ge(v_summed, m - 1)
                    if layer == 0:
                        pe.wait_ge(r_kept, m - 1)
                if layer == 0:
                    row_major(late_ps(0, p % 2), WRES, p)
                row_major(late_ps(1, p % 2), WV, p).then_inc(v_made, 1)

            def scores(layer, t, par, after_bank=None):
                n = t + layer * TILES
                pe.wait_ge(q_lo_ready, n + 1)
                if isinstance(t, int) and t == 0:
                    pe.wait_ge(q_kept, PAIRS * (layer + 1))
                    pe.wait_ge(k_lo_kept, PAIRS * (layer + 1))
                else:
                    pe.wait_ge(exped, n)
                for j in range(ROUNDS):
                    for i, (a, b) in enumerate(PARTS):
                        for cc in range(CC):
                            ins = nc.tensor.matmul(scores_ps[:, j, :], q_hl[:, par, a, cc, :],
                                                   k_hl[:, b, cc, j * BANK:(j + 1) * BANK],
                                                   start=(i == 0 and cc == 0), stop=(i == 2 and cc == CC - 1))
                    ins.then_inc(scored, 1)
                    if after_bank:
                        after_bank(j)

            def turn_round(n, par, j):
                pe.wait_ge(combined, n * ROUNDS + (j + 1))
                if isinstance(n, int) and n % TILES == 0 and j < 2:
                    pe.wait_ge(v_summed, (n // TILES + 1) * PAIRS)
                    pe.wait_ge(r_kept, PAIRS)
                if not isinstance(n, int) or n * ROUNDS + j >= 2:
                    pe.wait_ge(mix_lo, n * ROUNDS + (j - 1))
                for k in range(BLOCKS):
                    at = (BLOCKS * j + k) * P
                    ins = nc.tensor.transpose(turned_ps[:, j % 2, k * P:(k + 1) * P],
                                              mix[:, par, at:at + P], ident[:])
                ins.then_inc(turned, 1)

            def mix_round(n, par, j):
                pe.wait_ge(mix_lo, n * ROUNDS + (j + 1))
                if j == 0 and isinstance(n, int) and n % TILES == 0:
                    pe.wait_ge(v_lo_kept, (n // TILES + 1) * PAIRS)
                if j == 0 and (not isinstance(n, int) or n >= 1):
                    pe.wait_ge(y_ready, n)
                for bt in range(BLOCKS * j, BLOCKS * (j + 1)):
                    for i, (a, b) in enumerate(PARTS):
                        ins = nc.tensor.matmul(mixed_ps, mixT[:, par, a, bt, :],
                                               v_hl[:, b, bt * D:(bt + 1) * D],
                                               start=(bt == 0 and i == 0), stop=(bt == TILES - 1 and i == 2))
                if j == ROUNDS - 1:
                    ins.then_inc(mixed, 1)

            def turn_x1(t, par):
                pe.wait_ge(y_ready, t + 1)
                if not isinstance(t, int) or t >= 1:
                    pe.wait_ge(x1T_kept, t)
                for cc in range(CC):
                    ins = nc.tensor.transpose(x1T_ps[:, cc * P:(cc + 1) * P],
                                              y[:, par, cc * P:(cc + 1) * P], ident[:])
                ins.then_inc(x1_turned, 1)

            def step(layer, t, par, on):
                n = t + layer * TILES
                if isinstance(t, int) and t == 0:
                    if layer == 1:
                        pe.wait_ge(w_lo_done, 7)
                    for p in LATE[0]:
                        make_late(layer, p)
                if isinstance(t, int) and t == 2:
                    scores(layer, t, par, lambda j: turn_round(n - 2, par, j))
                elif on["tile"]:
                    scores(layer, t, par)
                if isinstance(t, int) and t < 2:
                    for p in LATE[t + 1]:
                        make_late(layer, p)
                    return
                tail = isinstance(t, int) and t >= TILES
                if layer == 0 and on["third"] and not tail:
                    turn_x1(t - 3, 1 - par)
                for j in range(ROUNDS):
                    if on["previous"]:
                        turn_round(n - 1, 1 - par, j)
                    if on["second"]:
                        mix_round(n - 2, par, j)
                if layer == 0 and tail and t == TILES + 2:
                    make_early(1, 3, 1)
                if layer == 0 and tail:
                    turn_x1(t - 3, 1 - par)
                if layer == 0 and isinstance(t, int) and t in NEXT_EARLY:
                    if t == TILES:
                        pe.wait_ge(exped, TILES)
                        pe.wait_ge(w_lo_done, 6)
                    for p in NEXT_EARLY[t]:
                        if p != 3:
                            make_early(1, p, p % 2)

            pe.wait_ge(w_lo_done, 1)
            make_early(0, 0, 0)
            make_early(0, 1, 1)
            with pe.Fori(1, PAIRS // 2) as i:
                for par in range(2):
                    make_early(0, i * 2 + par, par)
            pe.wait_ge(b_loaded, 5 * DMA)
            pe.wait_ge(w_lo_done, 4)
            for layer in range(LAYERS):
                over_steps(pe, lambda t, par, on, layer=layer: step(layer, t, par, on))


def kernel(**inputs):
    import numpy as np
    import concourse.bacc as bacc
    from concourse.bass_utils import run_bass_kernel_spmd

    nc = bacc.Bacc("TRN2", target_bir_lowering=False, num_devices=1)
    arrays = {}

    def dram(name, a):
        a = np.ascontiguousarray(a)
        arrays[name] = a
        return nc.dram_tensor(name, a.shape, mybir.dt.from_np(a.dtype), kind="ExternalInput").ap()

    w = {k[len("L0_gnn_"):]: np.asarray(v) for k, v in inputs.items() if k.startswith("L0_gnn_")}
    x = np.asarray(inputs["x"])
    x_ap = dram("x_rows", x)
    xT_ap = dram("x_columns", x.T)
    adj_ap = dram("adj", np.asarray(inputs["adj"]))
    weights = [[dram(f"{name}T", w[name].T) for name in names]
               for names in (("wk0", "wq0", "wv0", "wres"), ("wk1", "wq1", "wv1"))]
    cols = dram("bias_columns", np.stack([[w[f"b{n}{layer}"].reshape(D // P, P) for n in "qk"]
                                          for layer in range(LAYERS)]).transpose(3, 0, 1, 2))
    rows = [dram(name, w[name]) for name in ("bv0", "bres", "bv1")]
    ident = dram("identity", np.eye(P, dtype=np.float32))
    out = nc.dram_tensor("out", (N, D), F32, kind="ExternalOutput").ap()
    two_layer_attention(nc, x_ap, xT_ap, adj_ap, weights, cols, rows, ident, out)
    return run_bass_kernel_spmd(nc, [arrays], core_ids=[0]).results[0]["out"]
```
